# Optimizing a Trainium2 kernel written in Bass

```python
import numpy as np
import jax
import jax.numpy as jnp

def _softmax(x, axis=-1):
    return jax.nn.softmax(x, axis=axis)

def _gelu(x):
    return jax.nn.gelu(x, approximate=True)

def _silu(x):
    return jax.nn.silu(x)

def _sigmoid(x):
    return jax.nn.sigmoid(x)

def _layernorm(x, axis=-1, eps=1e-05):
    m = jnp.mean(x, axis=axis, keepdims=True)
    v = jnp.var(x, axis=axis, keepdims=True)
    return (x - m) / jnp.sqrt(v + eps)

def _scatter_add(tgt, idx, src, axis=0):
    return tgt.at[idx].add(src)

def _segment_sum(src, seg, n):
    return jax.ops.segment_sum(src, seg, n)
kernel_name = 'mk_adj_resnorm_d1_adj_r2_84101d'

def setup_inputs(seed: int=0):
    np.random.seed(seed)
    _w = jnp.asarray

    def _rec_inputs():
        import jax
        import jax.numpy as jnp
        _gk = jax.random.key(seed)
        x = -0.0005207 + 1.001 * jax.random.normal(jax.random.fold_in(_gk, 1), (4096, 128), jnp.float32)
        _a = jax.random.bernoulli(jax.random.fold_in(_gk, 2), 0.00195312, (4096, 4096))
        _a = jnp.logical_or(_a, jnp.swapaxes(_a, -1, -2))
        _a = jnp.logical_or(_a, jnp.eye(4096, dtype=bool))
        _af = _a.astype(jnp.float32)
        _af = _af * jax.random.uniform(jax.random.fold_in(_gk, 3), (4096, 4096), jnp.float32, 0.05, 5.41998)
        adj = _af
        return (x, adj)
    x, adj = _rec_inputs()

    def _L0_gnn_setup():
        import jax, jax.numpy as jnp
        import numpy as np
        N = 4096
        C = 128
        key = jax.random.key(seed)
        k1, k2, k3 = jax.random.split(key, 3)
        x = jax.random.normal(k1, (N, C), dtype=jnp.float32)
        evals = jax.random.uniform(k2, (N,), dtype=jnp.float32)
        evecs = jax.random.normal(k3, (N, N), dtype=jnp.float32)
        t = jnp.ones((1,), dtype=jnp.float32)
        return {'x': x, 'evals': evals, 'evecs': evecs, 't': t}
    _L0_gnn_all = _L0_gnn_setup()
    _L0_gnn_in = {k: v for k, v in _L0_gnn_all.items() if k in ('evals', 't')}
    del _L0_gnn_all
    return {'x': x, 'adj': adj, 'L0_gnn_evals': _L0_gnn_in['evals'], 'L0_gnn_t': _L0_gnn_in['t']}

def reference(x, adj, L0_gnn_evals, L0_gnn_t):
    import jax
    import jax.numpy as jnp

    def _L0_gnn_ref(x, evals, evecs, t):
        import jax, jax.numpy as jnp
        import numpy as np
        N = 4096
        C = 128
        t_eff = jnp.clip(t[0], 1e-08, None)
        x_spec = jnp.einsum('nk,nc->kc', evecs, x)
        coefs = jnp.exp(-evals * t_eff)[:, None]
        out = jnp.einsum('nk,kc->nc', evecs, coefs * x_spec)
        return out
    x = _layernorm(x + _L0_gnn_ref(x, L0_gnn_evals, adj, L0_gnn_t), axis=-1)
    return x

_drawn_inputs = setup_inputs


def setup_inputs(seed=0):
    import zlib

    import numpy as np

    out = dict(_drawn_inputs(seed))
    spreads = {}
    factors = {}
    for name, (base, spread) in spreads.items():
        noise = np.random.default_rng([zlib.crc32(name.encode()), seed]).standard_normal(out[name].shape)
        drawn = base * np.exp(spread * noise) if base else spread * noise
        out[name] = jnp.asarray(drawn.astype(out[name].dtype))
    for name, factor in factors.items():
        out[name] = (out[name] * factor).astype(out[name].dtype)
    return out
```

```python
from contextlib import ExitStack

import concourse.bass as bass
from concourse import mybir

F32 = mybir.dt.float32
F32R = mybir.dt.float32r
ACT = mybir.ActivationFunctionType
ALU = mybir.AluOpType

P = 128
N = 4096
C = 128
KB = 512
JT = KB // P
PAIR = 2 * P
GROUP = 2 * PAIR
BLOCKS = N // KB
PAIRS = N // PAIR
GROUPS = N // GROUP
QUARTERS = PAIRS // 4
RAW = 4
EPS = 1e-5
T_MIN = 1e-8


def build(nc, x, adj, evals, t, out):
    ctx = ExitStack()
    with ctx:
        def sb(name, shape, dt=F32):
            return ctx.enter_context(nc.sbuf_tensor(name, shape, dt))

        def pb(name, shape):
            return ctx.enter_context(nc.psum_tensor(name, shape, F32))

        def sem(name):
            return ctx.enter_context(nc.semaphore(name))

        raw = sb("raw", [P, RAW, 2, KB])
        a_hi = sb("a_hi", [P, 2, 2, KB], F32R)
        a_lo = sb("a_lo", [P, 2, 2, KB], F32R)
        x_in = sb("x_in", [P, N // P, C])
        x_hi = sb("x_hi", [P, 2, GROUP], F32R)
        x_lo = sb("x_lo", [P, 2, GROUP], F32R)
        at_hi = sb("at_hi", [P, JT, N], F32R)
        at_lo = sb("at_lo", [P, JT, N], F32R)
        xspec = sb("xspec", [P, KB])
        y_hi = sb("y_hi", [P, JT, C], F32R)
        y_lo = sb("y_lo", [P, JT, C], F32R)
        outT = sb("outT", [P, N])
        ident = sb("ident", [P, P])
        coef = sb("coef", [P, N // P])
        t_col = sb("t_col", [P, 1])
        neg_t = sb("neg_t", [P, 1])
        stat6 = sb("stat6", [P, 4, 6])
        mean_var = sb("mean_var", [P, 4, 2])
        var_eps = sb("var_eps", [P, 4])
        std = sb("std", [P, 4])
        rstd = sb("rstd", [P, 4])
        shift = sb("shift", [P, 4])

        ps_spec = pb("ps_spec", [P, KB])
        ps_y = pb("ps_y", [P, JT, C])
        ps_t = pb("ps_t", [P, 2, JT, PAIR])
        ps_out = pb("ps_out", [P, 2, GROUP])

        identity_zeroed = sem("identity_zeroed")
        identity_ready = sem("identity_ready")
        evals_loaded = sem("evals_loaded")
        t_loaded = sem("t_loaded")
        neg_t_ready = sem("neg_t_ready")
        evals_turned = sem("evals_turned")
        coef_ready = sem("coef_ready")
        x_first_loaded = sem("x_first_loaded")
        x_rest_loaded = sem("x_rest_loaded")
        raw_loaded = [sem(f"raw_loaded{i}") for i in range(RAW)]
        hi_ready = sem("hi_ready")
        lo_v_ready = sem("lo_v_ready")
        lo_g_ready = sem("lo_g_ready")
        x_hi_ready = sem("x_hi_ready")
        x_lo_ready = sem("x_lo_ready")
        spec_done = sem("spec_done")
        turned = sem("turned")
        at_hi_ready = sem("at_hi_ready")
        at_lo_ready = sem("at_lo_ready")
        xspec_ready = sem("xspec_ready")
        xspec_turned = sem("xspec_turned")
        y_full_ready = sem("y_full_ready")
        y_hi_ready = sem("y_hi_ready")
        y_ready = sem("y_ready")
        group_done = sem("group_done")
        group_added = sem("group_added")
        rows_turned = sem("rows_turned")
        stats_step = sem("stats_step")
        var_ready = sem("var_ready")
        std_ready = sem("std_ready")
        norm_ready = sem("norm_ready")
        normed = sem("normed")
        stored = [sem(f"stored{i}") for i in range(RAW)]

        adj_pairs = adj.rearrange("(r t p) k -> r p t k", t=2, p=P)
        x_tiles = x.rearrange("(m p) c -> p m c", p=P)
        out_groups = out.rearrange("(g m p) c -> g p m c", m=GROUP // P, p=P)
        FIRST_X = 2 * GROUP // P

        def final_bank(g):
            return ps_t[:, (g // 2) % 2, 2 * (g % 2):2 * (g % 2) + 2, :].rearrange("p j n -> p (j n)")

        def over_blocks(eng, quarter, unroll_first=False):
            for b, first, last in ((0, True, False), (None, False, False), (BLOCKS - 1, False, True)):
                if b is None:
                    with eng.Fori(1, BLOCKS - 1) as b:
                        quarter(b, 0, False, False)
                        with eng.Fori(1, QUARTERS - 1) as q:
                            quarter(b, q, False, False, inner=True)
                        quarter(b, QUARTERS - 1, False, False)
                else:
                    quarter(b, 0, first, last)
                    if first and unroll_first:
                        for q in range(1, QUARTERS - 1):
                            quarter(b, q, first, last, inner=True)
                    else:
                        with eng.Fori(1, QUARTERS - 1) as q:
                            quarter(b, q, first, last, inner=True)
                    quarter(b, QUARTERS - 1, first, last)

        block = ctx.enter_context(nc.Block())

        @block.sync
        def _(sp):
            for i in range(RAW):
                sp.dma_start(raw[:, i], adj_pairs[i, :, :, 0:KB]).then_inc(raw_loaded[i], 16)
                if i == 0:
                    sp.dma_start(x_in[:, 0:FIRST_X], x_tiles[:, 0:FIRST_X]).then_inc(x_first_loaded, 16)
            sp.dma_start(x_in[:, FIRST_X:], x_tiles[:, FIRST_X:]).then_inc(x_rest_loaded, 16)
            with sp.Fori(1, BLOCKS * QUARTERS) as u:
                b = u // QUARTERS
                q = u % QUARTERS
                for i in range(RAW):
                    sp.wait_ge(turned, u * 4 + (i - 3))
                    sp.wait_ge(lo_v_ready, u * 4 + (i - 3))
                    sp.wait_ge(lo_g_ready, u * 4 + (i - 3))
                    sp.dma_start(raw[:, i], adj_pairs[bass.ds(q * 4 + i, 1), :, :, bass.ds(b * KB, KB)]
                                 .rearrange("r p t k -> p (r t) k")).then_inc(raw_loaded[i], 16)
            for g in range(GROUPS):
                sp.wait_ge(normed, g + 1)
                sp.dma_start(out_groups[g], raw[:, g % RAW, 0].rearrange("p (m c) -> p m c", c=C))\
                    .then_inc(stored[g % RAW], 16)
            for s in stored:
                s_count = 16 * (GROUPS // RAW)
                sp.wait_ge(s, s_count)

        @block.scalar
        def _(act):
            act.dma_start(xspec[0:N // P, 0:P], evals.rearrange("(m p) -> m p", p=P)).then_inc(evals_loaded, 16)
            act.dma_start(t_col[:], t.rearrange("(a b) -> a b", a=1).to_broadcast([P, 1])).then_inc(t_loaded, 16)

            def round_pair(i):
                nc.scalar.activation(a_hi[:, i % 2], raw[:, i % RAW], ACT.Copy).then_inc(hi_ready, 1)

            for i in range(2):
                act.wait_ge(raw_loaded[i], 16)
                round_pair(i)
            act.wait_ge(evals_turned, 1)
            act.wait_ge(neg_t_ready, 1)
            nc.scalar.activation(coef[:], ps_y[:, 0, 0:N // P], ACT.Exp, scale=neg_t[:]).then_inc(coef_ready, 1)

            def take_spectrum(b):
                act.wait_ge(spec_done, b * PAIRS)
                if not isinstance(b, int) or b > 1:
                    act.wait_ge(y_ready, b - 1)
                nc.scalar.activation(xspec[:], ps_spec[:], ACT.Copy).then_inc(xspec_ready, 1)

            def quarter(b, q, first, last, inner=False):
                if not inner and q == 0 and not first:
                    take_spectrum(b)

                def round_ahead(i):
                    if last and not inner and q == QUARTERS - 1 and i >= 2:
                        return
                    act.wait_ge(raw_loaded[(i + 2) % RAW], (b * QUARTERS + q + (i + 2) // RAW + 1) * 16)
                    act.wait_ge(spec_done, b * PAIRS + q * 4 + (i + 1))
                    round_pair(i + 2)

                def take_turned(i):
                    act.wait_ge(turned, b * PAIRS + q * 4 + (i + 1))
                    if i % 2 == 0:
                        act.wait_ge(group_done, b * GROUPS + q * 2 + (i // 2 + 1))
                    nc.scalar.activation(at_hi[:, :, bass.ds(q * 4 * PAIR + i * PAIR, PAIR)],
                                         ps_t[:, i % 2], ACT.Copy).then_inc(at_hi_ready, 1)

                for i in range(4):
                    if not inner and q == 0 and i < 2:
                        round_ahead(i)
                        take_turned(i)
                    else:
                        take_turned(i)
                        round_ahead(i)

            over_blocks(act, quarter)
            take_spectrum(BLOCKS)

            for g in range(GROUPS):
                act.wait_ge(var_ready, g + 1)
                nc.scalar.activation(std[:], var_eps[:], ACT.Sqrt).then_inc(std_ready, 1)
                act.wait_ge(norm_ready, g + 1)
                if g >= RAW:
                    act.wait_ge(stored[g % RAW], 16 * (g // RAW))
                for m in range(4):
                    last = nc.scalar.activation(raw[:, g % RAW, 0, m * C:(m + 1) * C],
                                                final_bank(g)[:, m * C:(m + 1) * C], ACT.Identity,
                                                bias=shift[:, m:m + 1], scale=rstd[:, m:m + 1])
                last.then_inc(normed, 1)

        @block.gpsimd
        def _(pool):
            nc.gpsimd.memset(ident[:], 0.0).then_inc(identity_zeroed, 1)
            pool.wait_ge(identity_zeroed, 1)
            nc.gpsimd.affine_select(out=ident[:], in_=ident[:], compare_op=ALU.not_equal, fill=1.0, base=0,
                                    pattern=[[-1, P]], channel_multiplier=1).then_inc(identity_ready, 1)

            def low_half(i):
                nc.gpsimd.tensor_tensor(a_lo[:, i % 2, 1], raw[:, i % RAW, 1], a_hi[:, i % 2, 1].bitcast(F32),
                                        ALU.subtract).then_inc(lo_g_ready, 1)

            def low_x(g, slot):
                nc.gpsimd.tensor_tensor(x_lo[:, slot].rearrange("p (m c) -> p m c", c=C),
                                        x_in[:, bass.ds(g * 4, 4)],
                                        x_hi[:, slot].bitcast(F32).rearrange("p (m c) -> p m c", c=C),
                                        ALU.subtract).then_inc(x_lo_ready, 1)

            pool.wait_ge(hi_ready, 1)
            low_half(0)
            pool.wait_ge(x_hi_ready, 1)
            low_x(0, 0)
            pool.wait_ge(hi_ready, 2)
            low_half(1)

            def quarter(b, q, first, last, inner=False):
                for i in range(4):
                    if not (last and not inner and q == QUARTERS - 1 and i >= 2):
                        pool.wait_ge(hi_ready, b * PAIRS + q * 4 + (i + 3))
                        low_half(i + 2)
                        if i % 2 == 0:
                            pool.wait_ge(x_hi_ready, b * GROUPS + q * 2 + (i // 2 + 2))
                            low_x((q * 2 + (i // 2 + 1)) % GROUPS, (i // 2 + 1) % 2)

            over_blocks(pool, quarter)

        @block.vector
        def _(dve):
            dve.wait_ge(t_loaded, 16)
            nc.vector.tensor_scalar(neg_t[:], t_col[:], T_MIN, -1.0, ALU.max, ALU.mult).then_inc(neg_t_ready, 1)

            def low_half(i):
                nc.vector.tensor_tensor(a_lo[:, i % 2, 0], raw[:, i % RAW, 0], a_hi[:, i % 2, 0].bitcast(F32),
                                        ALU.subtract).then_inc(lo_v_ready, 1)

            def round_x(g, slot):
                nc.vector.tensor_copy(x_hi[:, slot].rearrange("p (m c) -> p m c", c=C),
                                      x_in[:, bass.ds(g * 4, 4)]).then_inc(x_hi_ready, 1)

            dve.wait_ge(x_first_loaded, 16)
            round_x(0, 0)
            dve.wait_ge(hi_ready, 1)
            low_half(0)
            dve.wait_ge(hi_ready, 2)
            low_half(1)

            def make_y(b):
                dve.wait_ge(xspec_turned, b)
                scale = coef[:, bass.ds((b - 1) * JT, JT)].unsqueeze(2).to_broadcast([P, JT, C])
                full = xspec[:].rearrange("p (j c) -> p j c", c=C)
                nc.vector.tensor_tensor(full, ps_y[:], scale, ALU.mult).then_inc(y_full_ready, 1)
                dve.wait_ge(y_full_ready, b)
                nc.vector.tensor_copy(y_hi[:], full).then_inc(y_hi_ready, 1)
                dve.wait_ge(y_hi_ready, b)
                nc.vector.tensor_tensor(y_lo[:], full, y_hi[:].bitcast(F32), ALU.subtract).then_inc(y_ready, 1)

            def add_group(b, g, bank, seed):
                dve.wait_ge(group_done, b * GROUPS + g + 1)
                sums = outT[:, bass.ds(g * GROUP, GROUP)]
                if seed:
                    nc.vector.tensor_copy(sums, ps_out[:, bank]).then_inc(group_added, 1)
                else:
                    dve.wait_ge(group_added, b * GROUPS + g - (GROUPS - 1))
                    nc.vector.tensor_tensor(sums, sums, ps_out[:, bank], ALU.add).then_inc(group_added, 1)

            def quarter(b, q, first, last, inner=False):
                start = not inner and q == 0
                if start and first:
                    dve.wait_ge(coef_ready, 1)
                if start and not first:
                    make_y(b)

                def low_ahead(i):
                    if last and not inner and q == QUARTERS - 1 and i >= 2:
                        return
                    dve.wait_ge(hi_ready, b * PAIRS + q * 4 + (i + 3))
                    low_half(i + 2)
                    if i % 2 == 0:
                        if start and first and i == 2:
                            dve.wait_ge(x_rest_loaded, 16)
                        round_x((q * 2 + (i // 2 + 1)) % GROUPS, (i // 2 + 1) % 2)

                def take_turned(i):
                    dve.wait_ge(at_hi_ready, b * PAIRS + q * 4 + (i + 1))
                    cols = bass.ds(q * 4 * PAIR + i * PAIR, PAIR)
                    nc.vector.tensor_tensor(at_lo[:, :, cols], ps_t[:, i % 2], at_hi[:, :, cols].bitcast(F32),
                                            ALU.subtract).then_inc(at_lo_ready, 1)

                for i in range(4):
                    if start and i < 2:
                        low_ahead(i)
                        add_group(b, i, i, first)
                        take_turned(i)
                    else:
                        if not start and i % 2 == 0:
                            add_group(b, q * 2 + i // 2, i // 2, first)
                        take_turned(i)
                        low_ahead(i)

            over_blocks(dve, quarter)
            make_y(BLOCKS)

            def row_norm(g):
                dve.wait_ge(rows_turned, g + 1)
                for m in range(4):
                    s = nc.vector.bn_stats(stat6[:, m, :], final_bank(g)[:, m * C:(m + 1) * C])
                s.then_inc(stats_step, 1)
                dve.wait_ge(stats_step, 3 * g + 1)
                for m in range(4):
                    s = nc.vector.bn_aggr(mean_var[:, m, :], stat6[:, m, :])
                s.then_inc(stats_step, 1)
                dve.wait_ge(stats_step, 3 * g + 2)
                nc.vector.tensor_scalar_add(var_eps[:], mean_var[:, :, 1], EPS).then_inc(var_ready, 1)
                dve.wait_ge(std_ready, g + 1)
                if g >= 1:
                    dve.wait_ge(normed, g)
                nc.vector.reciprocal(rstd[:], std[:]).then_inc(stats_step, 1)
                dve.wait_ge(stats_step, 3 * g + 3)
                nc.vector.scalar_tensor_tensor(out=shift[:], in0=mean_var[:, :, 0], scalar=-1.0, in1=rstd[:],
                                               op0=ALU.mult, op1=ALU.mult).then_inc(norm_ready, 1)

            for g in range(GROUPS):
                add_group(BLOCKS, g, g % 2, False)
                if g >= 1:
                    row_norm(g - 1)
            row_norm(GROUPS - 1)

        @block.tensor
        def _(pe):
            pe.wait_ge(identity_ready, 1)
            pe.wait_ge(evals_loaded, 16)
            nc.tensor.transpose(ps_y[:, 0, 0:N // P], xspec[0:N // P, 0:P], ident[0:N // P, 0:N // P])\
                .then_inc(evals_turned, 1)

            def turn_pair(i):
                for n in range(2):
                    for j in range(JT):
                        last = nc.tensor.transpose(ps_t[:, i % 2, j, n * P:(n + 1) * P],
                                                   raw[:, i % RAW, n, j * P:(j + 1) * P], ident[:])
                last.then_inc(turned, 1)

            def spectrum(b, q, i, opens, closes):
                count = b * PAIRS + q * 4 + (i + 1)
                pe.wait_ge(x_lo_ready, b * GROUPS + q * 2 + (i // 2 + 1))
                pe.wait_ge(lo_v_ready, count)
                pe.wait_ge(lo_g_ready, count)
                for n in range(2):
                    tile = slice(((i % 2) * 2 + n) * P, ((i % 2) * 2 + n + 1) * P)
                    hi, lo = x_hi[:, i // 2, tile], x_lo[:, i // 2, tile]
                    nc.tensor.matmul(ps_spec[:], hi, a_hi[:, i % 2, n], start=opens and n == 0, stop=False)
                    nc.tensor.matmul(ps_spec[:], hi, a_lo[:, i % 2, n], start=False, stop=False)
                    last = nc.tensor.matmul(ps_spec[:], lo, a_hi[:, i % 2, n], start=False,
                                            stop=closes and n == 1)
                last.then_inc(spec_done, 1)

            def synthesis_half(b, g, bank, half, seed, new=True):
                if half == 0 and new:
                    pe.wait_ge(group_added, b * GROUPS + g - 1)
                if seed:
                    for m in range(2 * half, 2 * half + 2):
                        last = nc.tensor.transpose(ps_out[:, bank, m * P:(m + 1) * P], x_in[:, g * 4 + m, :],
                                                   ident[:])
                else:
                    if half == 0:
                        pe.wait_ge(y_ready, b)
                        pe.wait_ge(at_lo_ready, (b - 1) * PAIRS + g * 2 + 2)
                    cols = bass.ds(g * GROUP, GROUP)
                    for j in range(2 * half, 2 * half + 2):
                        nc.tensor.matmul(ps_out[:, bank], y_hi[:, j], at_hi[:, j, cols], start=j == 0, stop=False)
                        nc.tensor.matmul(ps_out[:, bank], y_hi[:, j], at_lo[:, j, cols], start=False, stop=False)
                        last = nc.tensor.matmul(ps_out[:, bank], y_lo[:, j], at_hi[:, j, cols], start=False,
                                                stop=j == JT - 1)
                if half == 1:
                    last.then_inc(group_done, 1)

            def turn_spectrum(b):
                pe.wait_ge(xspec_ready, b)
                for j in range(JT):
                    last = nc.tensor.transpose(ps_y[:, j], xspec[:, j * P:(j + 1) * P], ident[:])
                last.then_inc(xspec_turned, 1)

            for i in range(2):
                pe.wait_ge(raw_loaded[i], 16)
                turn_pair(i)

            def quarter(b, q, first, last, inner=False):
                start = not inner and q == 0
                end = not inner and q == QUARTERS - 1

                def turn_ahead(i):
                    if end and last and i >= 2:
                        return
                    pe.wait_ge(raw_loaded[(i + 2) % RAW], (b * QUARTERS + q + (i + 2) // RAW + 1) * 16)
                    pe.wait_ge(at_lo_ready, b * PAIRS + q * 4 + (i + 1))
                    turn_pair(i + 2)

                if start and not first:
                    turn_spectrum(b)
                for i in range(4):
                    spectrum(b, q, i, start and i == 0, end and i == 3)
                    if start and i == 0:
                        continue
                    if start and i == 1:
                        if first:
                            pe.wait_ge(x_first_loaded, 16)
                        for half in range(4):
                            synthesis_half(b, half // 2, half // 2, half % 2, first, new=not first)
                        turn_ahead(0)
                        continue
                    if start and i == 2 and first:
                        pe.wait_ge(x_rest_loaded, 16)
                    if not (end and i >= 2):
                        h = (i + 2) // 2
                        synthesis_half(b, q * 2 + h, h % 2, i % 2, first)
                    if start and i == 2:
                        turn_ahead(1)
                    turn_ahead(i)

            over_blocks(pe, quarter, unroll_first=True)
            turn_spectrum(BLOCKS)

            def turn_rows(g):
                pe.wait_ge(group_added, BLOCKS * GROUPS + g + 1)
                if g >= 4:
                    pe.wait_ge(normed, g - 3)
                for m in range(4):
                    lo = g * GROUP + m * P
                    last = nc.tensor.transpose(final_bank(g)[:, m * P:(m + 1) * P], outT[:, lo:lo + P], ident[:])
                last.then_inc(rows_turned, 1)

            for g in range(GROUPS):
                for half in range(2):
                    synthesis_half(BLOCKS, g, g % 2, half, False)
                if g >= 1:
                    turn_rows(g - 1)
            turn_rows(GROUPS - 1)


_INS = ["x", "adj", "L0_gnn_evals", "L0_gnn_t"]


def kernel(**inputs):
    import numpy as np
    import concourse.bacc as bacc
    from concourse.bass_utils import run_bass_kernel_spmd

    nc = bacc.Bacc("TRN2", target_bir_lowering=False, num_devices=1)
    arrays, args = {}, []
    for name in _INS:
        a = np.ascontiguousarray(inputs[name])
        arrays[f"in_{name}"] = a
        args.append(nc.dram_tensor(f"in_{name}", a.shape, mybir.dt.from_np(a.dtype), kind="ExternalInput").ap())
    result = nc.dram_tensor("out_0", (N, C), F32, kind="ExternalOutput").ap()
    build(nc, *args, result)
    return run_bass_kernel_spmd(nc, [arrays], core_ids=[0]).results[0]["out_0"]
```

```python
from contextlib import ExitStack

import concourse.bass as bass
from concourse import mybir

F32 = mybir.dt.float32
F32R = mybir.dt.float32r
ACT = mybir.ActivationFunctionType
ALU = mybir.AluOpType

P = 128
SQ = 32
N = 4096
C = 128
KB = 512
JT = KB // P
PAIR = 2 * P
GROUP = 2 * PAIR
BLOCKS = N // KB
GROUPS = N // GROUP
QUARTERS = GROUPS // 2
RAW = 4
ROW_SLOTS = 4
V_COLS = 448
EPS = 1e-5
T_MIN = 1e-8
ODD_AT = [2, 4, 6, 7]
LAST_ORDER = [0, 2, 1, 4, 3, 6, 5, 7]


def build(nc, x, adj, evals, t, out):
    ctx = ExitStack()
    with ctx:
        def sb(name, shape, dt=F32):
            return ctx.enter_context(nc.sbuf_tensor(name, shape, dt))

        def pb(name, shape):
            return ctx.enter_context(nc.psum_tensor(name, shape, F32))

        def sem(name):
            return ctx.enter_context(nc.semaphore(name))

        raw = sb("raw", [P, RAW, 2 * KB])
        a_hi = sb("a_hi", [P, 2, 2 * KB], F32R)
        a_lo = sb("a_lo", [P, 2, 2 * KB], F32R)
        x_hi = sb("x_hi", [P, N // P * C], F32R)
        x_lo = sb("x_lo", [P, N // P * C], F32R)
        at_hi = sb("at_hi", [P, JT, QUARTERS * GROUP], F32R)
        at_lo = sb("at_lo", [P, JT, QUARTERS * GROUP], F32R)
        b_raw = sb("b_raw", [P, 2, 2 * KB])
        b_sq = sb("b_sq", [P, 2, JT, PAIR])
        bt_hi = sb("bt_hi", [P, JT, GROUP], F32R)
        bt_lo = sb("bt_lo", [P, JT, GROUP], F32R)
        bt_hi_pairs = bt_hi[:].rearrange("p (i j) n -> p i (j n)", i=2)
        bt_lo_pairs = bt_lo[:].rearrange("p (i j) n -> p i (j n)", i=2)
        xspec = sb("xspec", [P, KB])
        y_full = xspec[:].rearrange("p (j c) -> p j c", c=C)
        y_hi = sb("y_hi", [P, JT, C], F32R)
        y_lo = sb("y_lo", [P, JT, C], F32R)
        outT = sb("outT", [P, N])
        ident = sb("ident", [P, P])
        coef = sb("coef", [P, N // P])
        t_col = sb("t_col", [P, 1])
        neg_t = sb("neg_t", [P, 1])
        stat6 = sb("stat6", [P, 4, 6])
        mean_var = sb("mean_var", [P, 2, 4, 2])
        var_eps = sb("var_eps", [P, 2, 4])
        std = sb("std", [P, 2, 4])
        rstd = sb("rstd", [P, 2, 4])
        shift = sb("shift", [P, 2, 4])

        ps_spec = pb("ps_spec", [P, KB])
        ps_y = pb("ps_y", [P, JT, C])
        ps_t = pb("ps_t", [P, 2, JT, PAIR])
        ps_out = pb("ps_out", [P, 2, GROUP])

        identity_zeroed = sem("identity_zeroed")
        identity_ready = sem("identity_ready")
        evals_loaded = sem("evals_loaded")
        t_loaded = sem("t_loaded")
        neg_t_ready = sem("neg_t_ready")
        coef_ready = sem("coef_ready")
        x_loaded = [sem(f"x_loaded{n}") for n in range(QUARTERS)]
        x_turned = sem("x_turned")
        x_hi_ready = sem("x_hi_ready")
        x_lo_ready = sem("x_lo_ready")
        raw_loaded = [sem(f"raw_loaded{i}") for i in range(RAW)]
        hi_ready = sem("hi_ready")
        lo_v_ready = sem("lo_v_ready")
        lo_g_ready = sem("lo_g_ready")
        spec_done = sem("spec_done")
        turned = [sem(f"turned{k}") for k in range(2)]
        at_hi_ready = sem("at_hi_ready")
        at_lo_ready = sem("at_lo_ready")
        b_loaded = [sem(f"b_loaded{k}") for k in range(2)]
        c_loaded = [sem(f"c_loaded{k}") for k in range(2)]
        b_turned = sem("b_turned")
        bt_hi_ready = sem("bt_hi_ready")
        bt_lo_ready = [sem(f"bt_lo_ready{k}") for k in range(2)]
        xspec_ready = sem("xspec_ready")
        xspec_turned = sem("xspec_turned")
        y_full_ready = sem("y_full_ready")
        y_hi_ready = sem("y_hi_ready")
        y_ready = sem("y_ready")
        group_done = sem("group_done")
        group_added = sem("group_added")
        rows_turned = sem("rows_turned")
        stats_ready = sem("stats_ready")
        mean_ready = sem("mean_ready")
        var_ready = sem("var_ready")
        std_ready = sem("std_ready")
        rstd_ready = sem("rstd_ready")
        norm_ready = sem("norm_ready")
        normed = sem("normed")
        stored = [sem(f"stored{n}") for n in range(ROW_SLOTS)]

        adj_pairs = adj.rearrange("(r t p) k -> r p t k", t=2, p=P)
        adj_strips = adj.rearrange("(r s n) k -> r n s k", s=PAIR // SQ, n=SQ)
        x_quarters = x.rearrange("(g m p) c -> g p m c", g=QUARTERS, p=P)
        out_groups = out.rearrange("(g m p) c -> g p m c", m=GROUP // P, p=P)
        XQ = N // QUARTERS // P * C
        x_stage = [b_raw[:, 0], b_raw[:, 1],
                   b_sq[:, 0].rearrange("p j n -> p (j n)"), b_sq[:, 1].rearrange("p j n -> p (j n)")]

        def k_tiles(cols):
            return cols.rearrange("p (k j) -> p j k", j=JT)

        def final_bank(g):
            return ps_t[:, (g // 2) % 2, 2 * (g % 2):2 * (g % 2) + 2, :].rearrange("p j n -> p (j n)")

        def rows(s):
            return raw[:, 2 + s // 2 % 2, (s % 2) * GROUP:(s % 2 + 1) * GROUP]

        def a_slot(i, first):
            i = i % 4 if first else i % 2
            if i < 2:
                return a_hi[:, i], a_lo[:, i]
            return bt_hi_pairs[:, i - 2], bt_lo_pairs[:, i - 2]

        def strips_slot(o, k):
            return (raw if o % 2 else b_raw)[:, k]

        def odd_parts(o):
            if o % 2 == 0:
                return bt_hi[:], bt_lo[:]
            return tuple(m[:].rearrange("p i (j n) -> p (i j) n", n=GROUP) for m in (a_hi, a_lo))

        def over_blocks(eng, begin, quarter, unroll=False):
            def one(b, first, last):
                begin(b, first)
                if unroll:
                    for q in range(QUARTERS - 1):
                        quarter(b, q, first, last, False)
                else:
                    with eng.Fori(0, QUARTERS - 1) as q:
                        quarter(b, q, first, last, False)
                quarter(b, QUARTERS - 1, first, last, True)

            one(0, True, False)
            with eng.Fori(1, BLOCKS - 1) as b:
                one(b, False, False)
            one(BLOCKS - 1, False, True)

        block = ctx.enter_context(nc.Block())

        @block.sync
        def _(sp):
            def load_pair(i, b, q):
                sp.dma_start(raw[:, i].rearrange("p (t k) -> p t k", t=2),
                             adj_pairs[bass.ds(q * 4 + i, 1), :, :, bass.ds(b * KB, KB)]
                             .rearrange("r p t k -> p (r t) k")).then_inc(raw_loaded[i], 16)

            def load_strips(k, b, q, slot=None, loaded=b_loaded):
                slot = b_raw[:, k] if slot is None else slot
                strips = adj_strips[bass.ds(q * 4 + 2 + k, 1), :, :, bass.ds(b * KB, KB)]
                for a in range(P // SQ):
                    src = strips[:, :, :, a * P:(a + 1) * P]
                    sp.dma_start(slot[a * SQ:(a + 1) * SQ].rearrange("n (s c) -> n s c", c=P),
                                 src.rearrange("r n s c -> n (r s) c")).then_inc(loaded[k], 16)

            def load_quarter(u, strips=True):
                for i in range(RAW):
                    if i < 2 and strips:
                        sp.wait_ge(b_turned, u * 2 + (i - 9))
                        load_strips(i, u // QUARTERS - 1, u % QUARTERS)
                    sp.wait_ge(lo_v_ready, u * 4 + (i - 3))
                    sp.wait_ge(lo_g_ready, u * 4 + (i - 3))
                    if i < 2:
                        sp.wait_ge(turned[i], u)
                    load_pair(i, u // QUARTERS, u % QUARTERS)

            def load_x(n):
                sp.dma_start(x_stage[n].rearrange("p (m c) -> p m c", c=C), x_quarters[n])\
                    .then_inc(x_loaded[n], 16)

            for i in range(RAW):
                load_pair(i, 0, 0)
                if i == 0:
                    load_x(0)
            load_x(1)
            load_quarter(1, strips=False)
            load_x(2)
            load_x(3)
            load_quarter(2, strips=False)
            load_quarter(3, strips=False)
            sp.wait_ge(x_lo_ready, QUARTERS // 2)
            sp.wait_ge(x_turned, GROUPS // 2)
            for k in range(2):
                load_strips(k, 0, 0)
            for i in range(RAW):
                if i < 2:
                    sp.wait_ge(turned[i], QUARTERS)
                sp.wait_ge(lo_v_ready, 4 * QUARTERS + i - 3)
                sp.wait_ge(lo_g_ready, 4 * QUARTERS + i - 3)
                load_pair(i, 1, 0)
            with sp.Fori(QUARTERS + 1, BLOCKS * QUARTERS) as u:
                load_quarter(u)
            last = BLOCKS * QUARTERS
            for o in range(QUARTERS):
                for k in range(2):
                    if o == 1:
                        sp.wait_ge(lo_v_ready, last * 4 + (k - 3))
                        sp.wait_ge(lo_g_ready, last * 4 + (k - 3))
                        sp.wait_ge(turned[k], last)
                    else:
                        before = last + o - (1 if o == 0 else 2)
                        sp.wait_ge(b_turned, (before - QUARTERS) * 2 + k + 1)
                    load_strips(k, BLOCKS - 1, o, strips_slot(o, k), c_loaded if o % 2 else b_loaded)
            for s in range(GROUPS):
                sp.wait_ge(normed, s + 1)
                sp.dma_start(out_groups[LAST_ORDER[s]], rows(s).rearrange("p (m c) -> p m c", c=C))\
                    .then_inc(stored[s % ROW_SLOTS], 16)
            for n in range(ROW_SLOTS):
                sp.wait_ge(stored[n], 16 * GROUPS // ROW_SLOTS)

        @block.scalar
        def _(act):
            act.dma_start(coef[:].rearrange("p (b j) -> p b j", j=JT),
                          evals.rearrange("(b p j) -> p b j", p=P, j=JT)).then_inc(evals_loaded, 16)
            act.dma_start(t_col[:], t.rearrange("(a b) -> a b", a=1).to_broadcast([P, 1])).then_inc(t_loaded, 16)

            def round_pair(i, first):
                nc.scalar.activation(a_slot(i, first)[0], raw[:, i % RAW], ACT.Copy).then_inc(hi_ready, 1)

            for i in range(2):
                act.wait_ge(raw_loaded[i], 16)
                round_pair(i, True)
            act.wait_ge(evals_loaded, 16)
            act.wait_ge(neg_t_ready, 1)
            nc.scalar.activation(coef[:], coef[:], ACT.Exp, scale=neg_t[:]).then_inc(coef_ready, 1)

            def split_strips(b, q, k):
                act.wait_ge(b_turned, b * 8 + q * 2 + (k - 7))
                if k == 0:
                    act.wait_ge(group_added, b * GROUPS + q * 2)
                nc.scalar.activation(bt_hi[:, :, k * PAIR:(k + 1) * PAIR], b_sq[:, k], ACT.Copy)\
                    .then_inc(bt_hi_ready, 1)

            def quarter(b, q, first, last, end):
                def round_ahead(i):
                    act.wait_ge(raw_loaded[(i + 2) % RAW], (b * QUARTERS + q + (i + 2) // RAW + 1) * 16)
                    if not first:
                        act.wait_ge(spec_done, b * 16 + q * 4 + (i + 1))
                    elif q * 4 + i >= 2:
                        act.wait_ge(spec_done, q * 4 + i - 1)
                    round_pair(i + 2, first)

                for i in range(4):
                    if i < 2 and not first:
                        split_strips(b, q, i)
                    if i >= 2:
                        act.wait_ge(turned[i - 2], b * QUARTERS + q + 1)
                        if i == 2 and not first:
                            act.wait_ge(group_done, (b - 1) * GROUPS + q * 2 + 1)
                        nc.scalar.activation(at_hi[:, :, bass.ds(q * GROUP + (i - 2) * PAIR, PAIR)],
                                             ps_t[:, i - 2], ACT.Copy).then_inc(at_hi_ready, 1)
                    if end and i == 3:
                        act.wait_ge(spec_done, b * 16 + 16)
                        nc.scalar.activation(xspec[:], ps_spec[:], ACT.Copy).then_inc(xspec_ready, 1)
                    if not (last and end and i >= 2):
                        round_ahead(i)
                    if first and i < 2:
                        g = 2 * q + i
                        act.wait_ge(x_turned, g + 1)
                        nc.scalar.activation(outT[:, g * GROUP:(g + 1) * GROUP], ps_out[:, i], ACT.Copy)\
                            .then_inc(group_added, 1)

            for q in range(QUARTERS):
                quarter(0, q, True, False, q == QUARTERS - 1)
            with act.Fori(1, BLOCKS - 1) as b:
                with act.Fori(0, QUARTERS - 1) as q:
                    quarter(b, q, False, False, False)
                quarter(b, QUARTERS - 1, False, False, True)
            with act.Fori(0, QUARTERS - 1) as q:
                quarter(BLOCKS - 1, q, False, True, False)
            quarter(BLOCKS - 1, QUARTERS - 1, False, True, True)

            def odd_hi(o):
                if o == 0:
                    act.wait_ge(group_done, (BLOCKS - 1) * GROUPS)
                elif o >= 2:
                    act.wait_ge(group_done, (BLOCKS - 1) * GROUPS + ODD_AT[o - 2] + 1)
                for k in range(2):
                    act.wait_ge(b_turned, (BLOCKS - 1) * 8 + o * 2 + k + 1)
                    nc.scalar.activation(odd_parts(o)[0][:, :, k * PAIR:(k + 1) * PAIR], b_sq[:, k], ACT.Copy)\
                        .then_inc(bt_hi_ready, 1)

            def normalise(s):
                act.wait_ge(norm_ready, s + 1)
                if s >= ROW_SLOTS:
                    act.wait_ge(stored[s % ROW_SLOTS], 16 * (s // ROW_SLOTS))
                for m in range(4):
                    row = nc.scalar.activation(rows(s)[:, m * C:(m + 1) * C], final_bank(s)[:, m * C:(m + 1) * C],
                                               ACT.Identity, bias=shift[:, s % 2, m:m + 1],
                                               scale=rstd[:, s % 2, m:m + 1])
                row.then_inc(normed, 1)

            odd_hi(0)
            odd_hi(1)
            for s in range(GROUPS):
                act.wait_ge(var_ready, s + 1)
                nc.scalar.activation(std[:, s % 2], var_eps[:, s % 2], ACT.Sqrt).then_inc(std_ready, 1)
                normalise(s)
                if s in (1, 3):
                    odd_hi(2 + s // 2)

        @block.gpsimd
        def _(pool):
            nc.gpsimd.memset(ident[:], 0.0).then_inc(identity_zeroed, 1)
            pool.wait_ge(identity_zeroed, 1)
            nc.gpsimd.affine_select(out=ident[:], in_=ident[:], compare_op=ALU.not_equal, fill=1.0, base=0,
                                    pattern=[[-1, P]], channel_multiplier=1).then_inc(identity_ready, 1)

            def low_part(i, first):
                hi, lo = a_slot(i, first)
                nc.gpsimd.tensor_tensor(lo[:, V_COLS:], raw[:, i % RAW, V_COLS:], hi[:, V_COLS:].bitcast(F32),
                                        ALU.subtract).then_inc(lo_g_ready, 1)

            def low_x(n):
                pool.wait_ge(x_hi_ready, n + 1)
                cols = slice(n * XQ, (n + 1) * XQ)
                nc.gpsimd.tensor_tensor(x_lo[:, cols], x_stage[n], x_hi[:, cols].bitcast(F32), ALU.subtract)\
                    .then_inc(x_lo_ready, 1)

            pool.wait_ge(hi_ready, 1)
            low_part(0, True)
            low_x(0)
            pool.wait_ge(hi_ready, 2)
            low_part(1, True)

            def quarter(b, q, first, last, end):
                for i in range(2 if last and end else 4):
                    pool.wait_ge(hi_ready, b * 16 + q * 4 + (i + 3))
                    low_part(i + 2, first)
                    if first and i == 1 and not end:
                        low_x(q + 1)

            for q in range(QUARTERS):
                quarter(0, q, True, False, q == QUARTERS - 1)
            with pool.Fori(1, BLOCKS - 1) as b:
                with pool.Fori(0, QUARTERS) as q:
                    quarter(b, q, False, False, False)
            for q in range(QUARTERS):
                quarter(BLOCKS - 1, q, False, True, q == QUARTERS - 1)

            for o in range(QUARTERS):
                pool.wait_ge(bt_hi_ready, (BLOCKS - 1) * 8 + o * 2 + 1)
                hi, lo = odd_parts(o)
                nc.gpsimd.tensor_tensor(lo[:, :, :PAIR], b_sq[:, 0], hi[:, :, :PAIR].bitcast(F32),
                                        ALU.subtract).then_inc(bt_lo_ready[0], 1)

        @block.vector
        def _(dve):
            def low_part(i, first):
                hi, lo = a_slot(i, first)
                nc.vector.tensor_tensor(lo[:, :V_COLS], raw[:, i % RAW, :V_COLS], hi[:, :V_COLS].bitcast(F32),
                                        ALU.subtract).then_inc(lo_v_ready, 1)

            def round_x(n):
                dve.wait_ge(x_loaded[n], 16)
                nc.vector.tensor_copy(x_hi[:, n * XQ:(n + 1) * XQ], x_stage[n]).then_inc(x_hi_ready, 1)

            dve.wait_ge(t_loaded, 16)
            nc.vector.tensor_scalar(neg_t[:], t_col[:], T_MIN, -1.0, ALU.max, ALU.mult).then_inc(neg_t_ready, 1)
            round_x(0)
            dve.wait_ge(hi_ready, 1)
            low_part(0, True)
            dve.wait_ge(hi_ready, 2)
            low_part(1, True)
            dve.wait_ge(coef_ready, 1)

            def make_y(b):
                dve.wait_ge(xspec_turned, b)
                scale = coef[:, bass.ds((b - 1) * JT, JT)].unsqueeze(2).to_broadcast([P, JT, C])
                nc.vector.tensor_tensor(y_full, ps_y[:], scale, ALU.mult).then_inc(y_full_ready, 1)

            def split_y(b):
                dve.wait_ge(y_full_ready, b)
                nc.vector.tensor_copy(y_hi[:], y_full).then_inc(y_hi_ready, 1)
                dve.wait_ge(y_hi_ready, b)
                nc.vector.tensor_tensor(y_lo[:], y_full, y_hi[:].bitcast(F32), ALU.subtract).then_inc(y_ready, 1)

            def add_group(b, g, bank):
                dve.wait_ge(group_done, (b - 1) * GROUPS + g + 1)
                dve.wait_ge(group_added, b * GROUPS + g - (GROUPS - 1))
                sums = outT[:, bass.ds(g * GROUP, GROUP)]
                nc.vector.tensor_tensor(sums, sums, ps_out[:, bank], ALU.add).then_inc(group_added, 1)

            def turn_strips(b, q, k, begins=False):
                dve.wait_ge(b_loaded[k], (b * 4 + q - 3) * (16 * P // SQ))
                if begins:
                    dve.wait_ge(x_lo_ready, QUARTERS)
                    dve.wait_ge(x_turned, GROUPS)
                else:
                    dve.wait_ge(bt_lo_ready[k], b * 4 + q - 4)
                nc.vector.transpose(b_sq[:, k].rearrange("p j (s n) -> p s j n", n=SQ),
                                    b_raw[:, k].rearrange("p (s n j) -> p s j n", j=JT, n=SQ))\
                    .then_inc(b_turned, 1)

            def begin(b, first):
                if not first:
                    split_y(b)

            def quarter(b, q, first, last, end):
                def low_ahead(i):
                    dve.wait_ge(hi_ready, b * 16 + q * 4 + (i + 3))
                    low_part(i + 2, first)

                for i in range(4):
                    if i < 2 and not first:
                        dve.wait_ge(bt_hi_ready, b * 8 + q * 2 + (i - 7))
                        cols = slice(i * PAIR, (i + 1) * PAIR)
                        nc.vector.tensor_tensor(bt_lo[:, :, cols], b_sq[:, i], bt_hi[:, :, cols].bitcast(F32),
                                                ALU.subtract).then_inc(bt_lo_ready[i], 1)
                    if i == 2 and not first:
                        add_group(b, q * 2, 0)
                    if i >= 2:
                        dve.wait_ge(at_hi_ready, b * 8 + q * 2 + (i - 1))
                        cols = bass.ds(q * GROUP + (i - 2) * PAIR, PAIR)
                        nc.vector.tensor_tensor(at_lo[:, :, cols], ps_t[:, i - 2], at_hi[:, :, cols].bitcast(F32),
                                                ALU.subtract).then_inc(at_lo_ready, 1)
                    if end and i == 3:
                        turn_strips(b, q + 1, 1, begins=first)
                        if not first:
                            add_group(b, q * 2 + 1, 1)
                        make_y(b + 1)
                        if not last:
                            low_ahead(i)
                        continue
                    if not (last and end and i >= 2):
                        low_ahead(i)
                    if first and i == 1 and not end:
                        round_x(q + 1)
                    if i >= 2 and not (first and not end):
                        turn_strips(b, q + 1, i - 2, begins=first)
                    if i == 3 and not first:
                        add_group(b, q * 2 + 1, 1)

            for q in range(QUARTERS):
                quarter(0, q, True, False, q == QUARTERS - 1)
            with dve.Fori(1, BLOCKS - 1) as b:
                begin(b, False)
                with dve.Fori(0, QUARTERS - 1) as q:
                    quarter(b, q, False, False, False)
                quarter(b, QUARTERS - 1, False, False, True)
            begin(BLOCKS - 1, False)
            with dve.Fori(0, QUARTERS - 1) as q:
                quarter(BLOCKS - 1, q, False, True, False)
            quarter(BLOCKS - 1, QUARTERS - 1, False, True, True)
            split_y(BLOCKS)

            def turn_odd(o):
                for k in range(2):
                    dve.wait_ge((c_loaded if o % 2 else b_loaded)[k],
                                (o // 2 + 1 if o % 2 else (BLOCKS - 1) * 4 + o // 2 + 1) * (16 * P // SQ))
                    dve.wait_ge(bt_lo_ready[k], (BLOCKS - 1) * 4 + o)
                    nc.vector.transpose(b_sq[:, k].rearrange("p j (s n) -> p s j n", n=SQ),
                                        strips_slot(o, k).rearrange("p (s n j) -> p s j n", j=JT, n=SQ))\
                        .then_inc(b_turned, 1)

            def odd_lo(o):
                dve.wait_ge(bt_hi_ready, (BLOCKS - 1) * 8 + o * 2 + 2)
                hi, lo = odd_parts(o)
                nc.vector.tensor_tensor(lo[:, :, PAIR:], b_sq[:, 1], hi[:, :, PAIR:].bitcast(F32),
                                        ALU.subtract).then_inc(bt_lo_ready[1], 1)

            def add_last(s):
                dve.wait_ge(group_done, (BLOCKS - 1) * GROUPS + s + 1)
                dve.wait_ge(group_added, BLOCKS * GROUPS)
                g = LAST_ORDER[s]
                sums = outT[:, g * GROUP:(g + 1) * GROUP]
                nc.vector.tensor_tensor(sums, sums, ps_out[:, s % 2], ALU.add).then_inc(group_added, 1)

            def row_stats(g):
                dve.wait_ge(rows_turned, g + 1)
                if g >= 1:
                    dve.wait_ge(mean_ready, g)
                for m in range(4):
                    s = nc.vector.bn_stats(stat6[:, m, :], final_bank(g)[:, m * C:(m + 1) * C])
                s.then_inc(stats_ready, 1)

            def row_mean_var(g):
                dve.wait_ge(stats_ready, g + 1)
                for m in range(4):
                    s = nc.vector.bn_aggr(mean_var[:, g % 2, m, :], stat6[:, m, :])
                s.then_inc(mean_ready, 1)

            def row_var_eps(g):
                dve.wait_ge(mean_ready, g + 1)
                nc.vector.tensor_scalar_add(var_eps[:, g % 2], mean_var[:, g % 2, :, 1], EPS).then_inc(var_ready, 1)

            def row_rstd(g):
                dve.wait_ge(std_ready, g + 1)
                if g >= 2:
                    dve.wait_ge(normed, g - 1)
                nc.vector.reciprocal(rstd[:, g % 2], std[:, g % 2]).then_inc(rstd_ready, 1)

            def row_shift(g):
                dve.wait_ge(rstd_ready, g + 1)
                nc.vector.scalar_tensor_tensor(out=shift[:, g % 2], in0=mean_var[:, g % 2, :, 0], scalar=-1.0,
                                               in1=rstd[:, g % 2], op0=ALU.mult, op1=ALU.mult)\
                    .then_inc(norm_ready, 1)

            odd_lo(0)
            for s in range(GROUPS + 1):
                if s < GROUPS:
                    add_last(s)
                if s >= 1:
                    row_stats(s - 1)
                if s >= 2:
                    row_rstd(s - 2)
                if s >= 1:
                    row_mean_var(s - 1)
                if s >= 2:
                    row_shift(s - 2)
                if s >= 1:
                    row_var_eps(s - 1)
                if s in (0, 2, 4):
                    turn_odd(s // 2 + 1)
                if s in (1, 3, 5):
                    odd_lo(s // 2 + 1)
            row_rstd(GROUPS - 1)
            row_shift(GROUPS - 1)

        @block.tensor
        def _(pe):
            pe.wait_ge(identity_ready, 1)

            def turn_pair(i):
                for n in range(2):
                    tile = k_tiles(raw[:, i, n * KB:(n + 1) * KB])
                    for j in range(JT):
                        last = nc.tensor.transpose(ps_t[:, i, j, n * P:(n + 1) * P], tile[:, j], ident[:])
                last.then_inc(turned[i], 1)

            def spectrum(b, q, i):
                count = b * 16 + q * 4 + (i + 1)
                if isinstance(b, int) and b == 0:
                    pe.wait_ge(x_lo_ready, q + 1)
                pe.wait_ge(lo_v_ready, count)
                pe.wait_ge(lo_g_ready, count)
                hi, lo = a_slot(i, isinstance(b, int) and b == 0)
                for n in range(2):
                    tile = slice((q * 8 + i * 2 + n) * P, (q * 8 + i * 2 + n + 1) * P)
                    cols = slice(n * KB, (n + 1) * KB)
                    opens = q == 0 and i == 0 and n == 0
                    closes = q == QUARTERS - 1 and i == 3 and n == 1
                    nc.tensor.matmul(ps_spec[:], x_hi[:, tile], hi[:, cols], start=opens, stop=False)
                    nc.tensor.matmul(ps_spec[:], x_hi[:, tile], lo[:, cols], start=False, stop=False)
                    last = nc.tensor.matmul(ps_spec[:], x_lo[:, tile], hi[:, cols], start=False, stop=closes)
                last.then_inc(spec_done, 1)

            def synthesis_half(b, q, h, step=None):
                odd, half = h // 2, h % 2
                step = q * 2 + odd if step is None else step
                bank = step % 2
                if half == 0:
                    pe.wait_ge(group_added, b * GROUPS + step - 1)
                    pe.wait_ge(y_hi_ready, b)
                    if odd:
                        for k in range(2):
                            pe.wait_ge(bt_lo_ready[k], b * 4 + q - 3)
                    else:
                        pe.wait_ge(at_lo_ready, b * 8 + q * 2 - 6)
                if odd:
                    hi, lo = odd_parts(q if isinstance(b, int) and b == BLOCKS else 0)
                else:
                    hi, lo = (m[:, :, q * GROUP:(q + 1) * GROUP] for m in (at_hi, at_lo))
                js = range(2 * half, 2 * half + 2)
                for j in js:
                    nc.tensor.matmul(ps_out[:, bank], y_hi[:, j], hi[:, j], start=j == 0, stop=False)
                    nc.tensor.matmul(ps_out[:, bank], y_hi[:, j], lo[:, j], start=False, stop=False)
                if half == 0:
                    pe.wait_ge(y_ready, b)
                for j in js:
                    product = nc.tensor.matmul(ps_out[:, bank], y_lo[:, j], hi[:, j], start=False,
                                               stop=j == JT - 1)
                if half == 1:
                    product.then_inc(group_done, 1)

            def turn_spectrum(b):
                pe.wait_ge(xspec_ready, b)
                for j in range(JT):
                    last = nc.tensor.transpose(ps_y[:, j], k_tiles(xspec[:])[:, j], ident[:])
                last.then_inc(xspec_turned, 1)

            def turn_x(n):
                if n:
                    pe.wait_ge(group_added, 2 * n)
                for k in range(2):
                    for m in range(4):
                        lo = (k * 4 + m) * C
                        last = nc.tensor.transpose(ps_out[:, k, m * P:(m + 1) * P], x_stage[n][:, lo:lo + C],
                                                   ident[:])
                    last.then_inc(x_turned, 1)

            for i in range(2):
                pe.wait_ge(raw_loaded[i], 16)
                turn_pair(i)

            def begin(b, first):
                if not first:
                    turn_spectrum(b)

            def quarter(b, q, first, last, end):
                for i in range(4):
                    spectrum(b, q, i)
                    if first and i == 0:
                        pe.wait_ge(x_loaded[q], 16)
                        turn_x(q)
                    if not first:
                        for h in ([i] if q or i > 1 else [[], [0, 1]][i]):
                            synthesis_half(b, q, h)
                    if i >= 2 and not (last and end):
                        pe.wait_ge(raw_loaded[i - 2], (b * QUARTERS + q + 2) * 16)
                        pe.wait_ge(at_lo_ready, b * 8 + q * 2 + (i - 1))
                        turn_pair(i - 2)

            over_blocks(pe, begin, quarter, unroll=True)
            turn_spectrum(BLOCKS)

            def turn_rows(s):
                pe.wait_ge(group_added, BLOCKS * GROUPS + s + 1)
                if s >= 4:
                    pe.wait_ge(normed, s - 3)
                for m in range(4):
                    lo = LAST_ORDER[s] * GROUP + m * P
                    last = nc.tensor.transpose(final_bank(s)[:, m * P:(m + 1) * P], outT[:, lo:lo + P], ident[:])
                last.then_inc(rows_turned, 1)

            for s in range(GROUPS):
                g = LAST_ORDER[s]
                for half in range(2):
                    synthesis_half(BLOCKS, g // 2, 2 * (g % 2) + half, step=s)
                if s >= 1:
                    turn_rows(s - 1)
            turn_rows(GROUPS - 1)


_INS = ["x", "adj", "L0_gnn_evals", "L0_gnn_t"]


def kernel(**inputs):
    import numpy as np
    import concourse.bacc as bacc
    from concourse.bass_utils import run_bass_kernel_spmd

    nc = bacc.Bacc("TRN2", target_bir_lowering=False, num_devices=1)
    arrays, args = {}, []
    for name in _INS:
        a = np.ascontiguousarray(inputs[name])
        arrays[f"in_{name}"] = a
        args.append(nc.dram_tensor(f"in_{name}", a.shape, mybir.dt.from_np(a.dtype), kind="ExternalInput").ap())
    result = nc.dram_tensor("out_0", (N, C), F32, kind="ExternalOutput").ap()
    build(nc, *args, result)
    return run_bass_kernel_spmd(nc, [arrays], core_ids=[0]).results[0]["out_0"]
```

```python
from contextlib import ExitStack

import concourse.bass as bass
from concourse import mybir

F32 = mybir.dt.float32
F32R = mybir.dt.float32r
ACT = mybir.ActivationFunctionType
ALU = mybir.AluOpType

P = 128
SQ = 32
N = 4096
C = 128
KB = 512
JT = KB // P
PAIR = 2 * P
GROUP = 2 * PAIR
BLOCKS = N // KB
GROUPS = N // GROUP
QUARTERS = GROUPS // 2
RAW = 4
WARM = [19, 6]
ROW_SLOTS = 4
V_COLS = 448
EPS = 1e-5
T_MIN = 1e-8
LAST_ORDER = [0, 2, 1, 4, 3, 6, 5, 7]
GPSIMD_LO = [1, 2]


def build(nc, x, adj, evals, t, out):
    ctx = ExitStack()
    with ctx:
        def sb(name, shape, dt=F32):
            return ctx.enter_context(nc.sbuf_tensor(name, shape, dt))

        def pb(name, shape):
            return ctx.enter_context(nc.psum_tensor(name, shape, F32))

        def sem(name):
            return ctx.enter_context(nc.semaphore(name))

        raw = sb("raw", [P, RAW, 2 * KB])
        a_hi = sb("a_hi", [P, 2, 2 * KB], F32R)
        a_lo = sb("a_lo", [P, 2, 2 * KB], F32R)
        x_hi = sb("x_hi", [P, N // P * C], F32R)
        x_lo = sb("x_lo", [P, N // P * C], F32R)
        at_hi = sb("at_hi", [P, JT, QUARTERS * GROUP], F32R)
        at_lo = sb("at_lo", [P, JT, QUARTERS * GROUP], F32R)
        b_raw = sb("b_raw", [P, 2, 2 * KB])
        b_sq = sb("b_sq", [P, 2, JT, PAIR])
        bt_hi = sb("bt_hi", [P, JT, GROUP], F32R)
        bt_lo = sb("bt_lo", [P, JT, GROUP], F32R)
        bt_hi_pairs = bt_hi[:].rearrange("p (i j) n -> p i (j n)", i=2)
        bt_lo_pairs = bt_lo[:].rearrange("p (i j) n -> p i (j n)", i=2)
        xspec = sb("xspec", [P, KB])
        y_full = xspec[:].rearrange("p (j c) -> p j c", c=C)
        y_hi = sb("y_hi", [P, 2, JT, C], F32R)
        y_lo = sb("y_lo", [P, 2, JT, C], F32R)
        outT = sb("outT", [P, N])
        ident = sb("ident", [P, P])
        coef = sb("coef", [P, N // P])
        t_col = sb("t_col", [P, 1])
        neg_t = sb("neg_t", [P, 1])
        eps_col = sb("eps_col", [P, 1])
        stat6 = sb("stat6", [P, 4, 6])
        mean_var = sb("mean_var", [P, 2, 4, 2])
        std = sb("std", [P, 2, 4])
        rstd = sb("rstd", [P, 2, 4])
        shift = sb("shift", [P, 2, 4])

        ps_spec = pb("ps_spec", [P, KB])
        ps_y = pb("ps_y", [P, JT, C])
        ps_t = pb("ps_t", [P, 2, JT, PAIR])
        ps_out = pb("ps_out", [P, 2, GROUP])

        identity_zeroed = sem("identity_zeroed")
        identity_ready = sem("identity_ready")
        evals_loaded = sem("evals_loaded")
        t_loaded = sem("t_loaded")
        neg_t_ready = sem("neg_t_ready")
        coef_ready = sem("coef_ready")
        eps_ready = sem("eps_ready")
        x_loaded = [sem(f"x_loaded{n}") for n in range(QUARTERS)]
        x_turned = sem("x_turned")
        x_hi_ready = sem("x_hi_ready")
        x_lo_ready = sem("x_lo_ready")
        raw_loaded = [sem(f"raw_loaded{i}") for i in range(RAW)]
        hi_ready = sem("hi_ready")
        lo_v_ready = sem("lo_v_ready")
        lo_g_ready = sem("lo_g_ready")
        spec_done = sem("spec_done")
        turned = [sem(f"turned{k}") for k in range(2)]
        at_hi_ready = sem("at_hi_ready")
        at_lo_ready = sem("at_lo_ready")
        b_loaded = [sem(f"b_loaded{k}") for k in range(2)]
        c_loaded = [sem(f"c_loaded{k}") for k in range(2)]
        b_turned = sem("b_turned")
        bt_hi_ready = sem("bt_hi_ready")
        bt_lo_ready = [sem(f"bt_lo_ready{k}") for k in range(2)]
        xspec_ready = sem("xspec_ready")
        xspec_turned = sem("xspec_turned")
        y_full_ready = sem("y_full_ready")
        y_hi_ready = sem("y_hi_ready")
        y_ready = sem("y_ready")
        group_done = sem("group_done")
        group_added = sem("group_added")
        rows_turned = sem("rows_turned")
        stats_ready = sem("stats_ready")
        mean_ready = sem("mean_ready")
        std_ready = sem("std_ready")
        rstd_ready = sem("rstd_ready")
        norm_ready = sem("norm_ready")
        normed = sem("normed")
        last_normed = sem("last_normed")
        stored = [sem(f"stored{n}") for n in range(ROW_SLOTS)]

        adj_pairs = adj.rearrange("(r t p) k -> r p t k", t=2, p=P)
        adj_strips = adj.rearrange("(r s n) k -> r n s k", s=PAIR // SQ, n=SQ)
        x_quarters = x.rearrange("(g m p) c -> g p m c", g=QUARTERS, p=P)
        out_groups = out.rearrange("(g m p) c -> g p m c", m=GROUP // P, p=P)
        XQ = N // QUARTERS // P * C
        x_stage = [b_raw[:, 0], b_raw[:, 1],
                   b_sq[:, 0].rearrange("p j n -> p (j n)"), b_sq[:, 1].rearrange("p j n -> p (j n)")]

        def k_tiles(cols):
            return cols.rearrange("p (k j) -> p j k", j=JT)

        def final_bank(g):
            return ps_t[:, (g // 2) % 2, 2 * (g % 2):2 * (g % 2) + 2, :].rearrange("p j n -> p (j n)")

        def rows(s):
            return raw[:, 2 + s // 2 % 2, (s % 2) * GROUP:(s % 2 + 1) * GROUP]

        def y_slot(b):
            return 1 if isinstance(b, int) and b == BLOCKS else 0

        def a_slot(i, first):
            i = i % 4 if first else i % 2
            if i < 2:
                return a_hi[:, i], a_lo[:, i]
            return bt_hi_pairs[:, i - 2], bt_lo_pairs[:, i - 2]

        def strips_slot(o, k):
            return (raw if o % 2 else b_raw)[:, k]

        def odd_parts(o):
            if o == 0:
                return bt_hi[:], bt_lo[:]
            if o == 1:
                return tuple(m[:].rearrange("p i (j n) -> p (i j) n", n=GROUP) for m in (a_hi, a_lo))
            return tuple(m[:, :, (o - 2) * GROUP:(o - 1) * GROUP] for m in (at_hi, at_lo))

        block = ctx.enter_context(nc.Block())

        @block.sync
        def _(sp):
            def load_pair(i, b, q):
                sp.dma_start(raw[:, i].rearrange("p (t k) -> p t k", t=2),
                             adj_pairs[bass.ds(q * 4 + i, 1), :, :, bass.ds(b * KB, KB)]
                             .rearrange("r p t k -> p (r t) k")).then_inc(raw_loaded[i], 16)

            def load_strips(k, b, q, slot=None, loaded=b_loaded):
                slot = b_raw[:, k] if slot is None else slot
                strips = adj_strips[bass.ds(q * 4 + 2 + k, 1), :, :, bass.ds(b * KB, KB)]
                for a in range(P // SQ):
                    src = strips[:, :, :, a * P:(a + 1) * P]
                    sp.dma_start(slot[a * SQ:(a + 1) * SQ].rearrange("n (s c) -> n s c", c=P),
                                 src.rearrange("r n s c -> n (r s) c")).then_inc(loaded[k], 16)

            def load_quarter(u, strips=True):
                for i in range(RAW):
                    if i < 2 and strips:
                        sp.wait_ge(b_turned, u * 2 + (i - 9))
                        load_strips(i, u // QUARTERS - 1, u % QUARTERS)
                    sp.wait_ge(lo_v_ready, u * 4 + (i - 3))
                    sp.wait_ge(lo_g_ready, u * 4 + (i - 3))
                    if i < 2:
                        sp.wait_ge(turned[i], u)
                    load_pair(i, u // QUARTERS, u % QUARTERS)

            def load_x(n):
                sp.dma_start(x_stage[n].rearrange("p (m c) -> p m c", c=C), x_quarters[n])\
                    .then_inc(x_loaded[n], 16)

            load_x(0)
            for i in range(RAW):
                load_pair(i, 0, 0)
            load_x(1)
            sp.dma_start(coef[:].rearrange("p (b j) -> p b j", j=JT),
                         evals.rearrange("(b p j) -> p b j", p=P, j=JT)).then_inc(evals_loaded, 16)
            sp.dma_start(t_col[:], t.rearrange("(a b) -> a b", a=1).to_broadcast([P, 1])).then_inc(t_loaded, 16)
            load_quarter(1, strips=False)
            load_x(2)
            load_x(3)
            load_quarter(2, strips=False)
            load_quarter(3, strips=False)
            sp.wait_ge(x_lo_ready, QUARTERS // 2)
            sp.wait_ge(x_turned, GROUPS // 2)
            for k in range(2):
                load_strips(k, 0, 0)
            for i in range(RAW):
                if i < 2:
                    sp.wait_ge(turned[i], QUARTERS)
                sp.wait_ge(lo_v_ready, 4 * QUARTERS + i - 3)
                sp.wait_ge(lo_g_ready, 4 * QUARTERS + i - 3)
                load_pair(i, 1, 0)
            with sp.Fori(QUARTERS + 1, BLOCKS * QUARTERS) as u:
                load_quarter(u)
            last = BLOCKS * QUARTERS
            for o in range(QUARTERS):
                for k in range(2):
                    if o == 1:
                        sp.wait_ge(lo_v_ready, last * 4 + (k - 3))
                        sp.wait_ge(lo_g_ready, last * 4 + (k - 3))
                        sp.wait_ge(turned[k], last)
                    else:
                        before = last + o - (1 if o == 0 else 2)
                        sp.wait_ge(b_turned, (before - QUARTERS) * 2 + k + 1)
                    load_strips(k, BLOCKS - 1, o, strips_slot(o, k), c_loaded if o % 2 else b_loaded)
            for s in range(GROUPS):
                if s < GROUPS - 1:
                    sp.wait_ge(normed, s + 1)
                else:
                    sp.wait_ge(last_normed, 1)
                sp.dma_start(out_groups[LAST_ORDER[s]], rows(s).rearrange("p (m c) -> p m c", c=C))\
                    .then_inc(stored[s % ROW_SLOTS], 16)
            for n in range(ROW_SLOTS):
                sp.wait_ge(stored[n], 16 * GROUPS // ROW_SLOTS)

        @block.scalar
        def _(act):
            def round_pair(i, first):
                nc.scalar.activation(a_slot(i, first)[0], raw[:, i % RAW], ACT.Copy).then_inc(hi_ready, 1)

            for i in range(2):
                act.wait_ge(raw_loaded[i], 16)
                round_pair(i, True)

            def split_strips(b, q, k):
                act.wait_ge(b_turned, b * 8 + q * 2 + (k - 7))
                if k == 0:
                    act.wait_ge(group_added, b * GROUPS + q * 2)
                nc.scalar.activation(bt_hi[:, :, k * PAIR:(k + 1) * PAIR], b_sq[:, k], ACT.Copy)\
                    .then_inc(bt_hi_ready, 1)

            def quarter(b, q, first, last, end):
                def round_ahead(i):
                    act.wait_ge(raw_loaded[(i + 2) % RAW], (b * QUARTERS + q + (i + 2) // RAW + 1) * 16)
                    if not first:
                        act.wait_ge(spec_done, b * 16 + q * 4 + (i + 1))
                    elif q * 4 + i >= 2:
                        act.wait_ge(spec_done, q * 4 + i - 1)
                    round_pair(i + 2, first)

                for i in range(4):
                    if i < 2 and not first:
                        split_strips(b, q, i)
                    k = i if first else i - 2
                    if k in (0, 1):
                        act.wait_ge(turned[k], b * QUARTERS + q + 1)
                        if k == 0 and not first:
                            act.wait_ge(group_done, (b - 1) * GROUPS + q * 2 + 1)
                        nc.scalar.activation(at_hi[:, :, bass.ds(q * GROUP + k * PAIR, PAIR)], ps_t[:, k],
                                             ACT.Copy).then_inc(at_hi_ready, 1)
                    if end and i == 3:
                        act.wait_ge(spec_done, b * 16 + 16)
                        nc.scalar.activation(xspec[:], ps_spec[:], ACT.Copy).then_inc(xspec_ready, 1)
                    if not (last and end and i >= 2):
                        round_ahead(i)
                    if first and i in (1, 2):
                        g = 2 * q + i - 1
                        act.wait_ge(x_turned, g + 1)
                        nc.scalar.activation(outT[:, g * GROUP:(g + 1) * GROUP], ps_out[:, i - 1], ACT.Copy)\
                            .then_inc(group_added, 1)

            for q in range(QUARTERS):
                if q == 2:
                    act.wait_ge(evals_loaded, 16)
                    act.wait_ge(neg_t_ready, 1)
                    nc.scalar.activation(coef[:], coef[:], ACT.Exp, scale=neg_t[:]).then_inc(coef_ready, 1)
                quarter(0, q, True, False, q == QUARTERS - 1)
            with act.Fori(1, BLOCKS - 1) as b:
                with act.Fori(0, QUARTERS - 1) as q:
                    quarter(b, q, False, False, False)
                quarter(b, QUARTERS - 1, False, False, True)
            with act.Fori(0, QUARTERS - 1) as q:
                quarter(BLOCKS - 1, q, False, True, False)
            quarter(BLOCKS - 1, QUARTERS - 1, False, True, True)

            def odd_hi(o, k):
                if o != 1 and k == 0:
                    act.wait_ge(group_done, (BLOCKS - 1) * GROUPS + [0, None, 1, 2][o])
                act.wait_ge(b_turned, (BLOCKS - 1) * 8 + o * 2 + k + 1)
                nc.scalar.activation(odd_parts(o)[0][:, :, k * PAIR:(k + 1) * PAIR], b_sq[:, k], ACT.Copy)\
                    .then_inc(bt_hi_ready, 1)

            def normalise(s):
                act.wait_ge(norm_ready, s + 1)
                if s >= ROW_SLOTS:
                    act.wait_ge(stored[s % ROW_SLOTS], 16 * (s // ROW_SLOTS))
                for m in range(4):
                    row = nc.scalar.activation(rows(s)[:, m * C:(m + 1) * C], final_bank(s)[:, m * C:(m + 1) * C],
                                               ACT.Identity, bias=shift[:, s % 2, m:m + 1],
                                               scale=rstd[:, s % 2, m:m + 1])
                row.then_inc(normed, 1)

            for o in range(2):
                for k in range(2):
                    odd_hi(o, k)
            act.wait_ge(eps_ready, 1)
            for s in range(GROUPS):
                act.wait_ge(mean_ready, s + 1)
                nc.scalar.activation(std[:, s % 2], mean_var[:, s % 2, :, 1], ACT.Sqrt, bias=eps_col[:])\
                    .then_inc(std_ready, 1)
                for k in {0: [0, 1], 1: [0], 2: [1]}.get(s, []):
                    odd_hi(2 + min(s, 1), k)
                if s >= 1:
                    normalise(s - 1)

        @block.gpsimd
        def _(pool):
            nc.gpsimd.memset(ident[:], 0.0).then_inc(identity_zeroed, 1)
            pool.wait_ge(identity_zeroed, 1)
            nc.gpsimd.affine_select(out=ident[:], in_=ident[:], compare_op=ALU.not_equal, fill=1.0, base=0,
                                    pattern=[[-1, P]], channel_multiplier=1).then_inc(identity_ready, 1)

            def low_part(i, first):
                hi, lo = a_slot(i, first)
                nc.gpsimd.tensor_tensor(lo[:, V_COLS:], raw[:, i % RAW, V_COLS:], hi[:, V_COLS:].bitcast(F32),
                                        ALU.subtract).then_inc(lo_g_ready, 1)

            pool.wait_ge(hi_ready, 1)
            low_part(0, True)
            pool.wait_ge(hi_ready, 2)
            low_part(1, True)

            def quarter(b, q, first, last, end):
                for i in range(2 if last and end else 4):
                    pool.wait_ge(hi_ready, b * 16 + q * 4 + (i + 3))
                    low_part(i + 2, first)

            for q in range(QUARTERS):
                quarter(0, q, True, False, q == QUARTERS - 1)
            with pool.Fori(1, BLOCKS - 1) as b:
                with pool.Fori(0, QUARTERS) as q:
                    quarter(b, q, False, False, False)
            for q in range(QUARTERS):
                quarter(BLOCKS - 1, q, False, True, q == QUARTERS - 1)

            for o in range(QUARTERS):
                hi, lo = odd_parts(o)
                for k in range(2 if o in GPSIMD_LO else 1):
                    pool.wait_ge(bt_hi_ready, (BLOCKS - 1) * 8 + o * 2 + k + 1)
                    cols = slice(k * PAIR, (k + 1) * PAIR)
                    nc.gpsimd.tensor_tensor(lo[:, :, cols], b_sq[:, k], hi[:, :, cols].bitcast(F32),
                                            ALU.subtract).then_inc(bt_lo_ready[k], 1)

        @block.vector
        def _(dve):
            def low_part(i, first):
                hi, lo = a_slot(i, first)
                nc.vector.tensor_tensor(lo[:, :V_COLS], raw[:, i % RAW, :V_COLS], hi[:, :V_COLS].bitcast(F32),
                                        ALU.subtract).then_inc(lo_v_ready, 1)

            def round_x(n):
                dve.wait_ge(x_loaded[n], 16)
                nc.vector.tensor_copy(x_hi[:, n * XQ:(n + 1) * XQ], x_stage[n]).then_inc(x_hi_ready, 1)

            def low_x(n):
                dve.wait_ge(x_hi_ready, n + 1)
                cols = slice(n * XQ, (n + 1) * XQ)
                nc.vector.tensor_tensor(x_lo[:, cols], x_stage[n], x_hi[:, cols].bitcast(F32), ALU.subtract)\
                    .then_inc(x_lo_ready, 1)

            nc.vector.memset(eps_col[:], EPS).then_inc(eps_ready, 1)
            round_x(0)
            dve.wait_ge(hi_ready, 1)
            low_part(0, True)
            low_x(0)
            dve.wait_ge(hi_ready, 2)
            low_part(1, True)

            def make_y(b):
                dve.wait_ge(xspec_turned, b)
                scale = coef[:, bass.ds((b - 1) * JT, JT)].unsqueeze(2).to_broadcast([P, JT, C])
                nc.vector.tensor_tensor(y_full, ps_y[:], scale, ALU.mult).then_inc(y_full_ready, 1)

            def split_y(b):
                dve.wait_ge(y_full_ready, b)
                hi, lo = y_hi[:, y_slot(b)], y_lo[:, y_slot(b)]
                nc.vector.tensor_copy(hi, y_full).then_inc(y_hi_ready, 1)
                dve.wait_ge(y_hi_ready, b)
                nc.vector.tensor_tensor(lo, y_full, hi.bitcast(F32), ALU.subtract).then_inc(y_ready, 1)

            def add_group(b, g, bank):
                dve.wait_ge(group_done, (b - 1) * GROUPS + g + 1)
                dve.wait_ge(group_added, b * GROUPS + g - (GROUPS - 1))
                sums = outT[:, bass.ds(g * GROUP, GROUP)]
                nc.vector.tensor_tensor(sums, sums, ps_out[:, bank], ALU.add).then_inc(group_added, 1)

            def turn_strips(b, q, k, begins=False):
                dve.wait_ge(b_loaded[k], (b * 4 + q - 3) * (16 * P // SQ))
                if begins:
                    dve.wait_ge(x_lo_ready, QUARTERS)
                    dve.wait_ge(x_turned, GROUPS)
                else:
                    dve.wait_ge(bt_lo_ready[k], b * 4 + q - 4)
                nc.vector.transpose(b_sq[:, k].rearrange("p j (s n) -> p s j n", n=SQ),
                                    b_raw[:, k].rearrange("p (s n j) -> p s j n", j=JT, n=SQ))\
                    .then_inc(b_turned, 1)

            def begin(b, first):
                if not first:
                    make_y(b)
                    split_y(b)

            def quarter(b, q, first, last, end):
                def low_ahead(i):
                    dve.wait_ge(hi_ready, b * 16 + q * 4 + (i + 3))
                    low_part(i + 2, first)

                for i in range(4):
                    if i < 2 and not first:
                        dve.wait_ge(bt_hi_ready, b * 8 + q * 2 + (i - 7))
                        cols = slice(i * PAIR, (i + 1) * PAIR)
                        nc.vector.tensor_tensor(bt_lo[:, :, cols], b_sq[:, i], bt_hi[:, :, cols].bitcast(F32),
                                                ALU.subtract).then_inc(bt_lo_ready[i], 1)
                    if i == 2 and not first:
                        add_group(b, q * 2, 0)
                    k = i if first else i - 2
                    if k in (0, 1):
                        dve.wait_ge(at_hi_ready, b * 8 + q * 2 + (k + 1))
                        cols = bass.ds(q * GROUP + k * PAIR, PAIR)
                        nc.vector.tensor_tensor(at_lo[:, :, cols], ps_t[:, k], at_hi[:, :, cols].bitcast(F32),
                                                ALU.subtract).then_inc(at_lo_ready, 1)
                    if end and i == 3:
                        turn_strips(b, q + 1, 1, begins=first)
                        if not first and not last:
                            add_group(b, q * 2 + 1, 1)
                        if not last:
                            low_ahead(i)
                        continue
                    if not (last and end and i >= 2):
                        low_ahead(i)
                    if first and i == 1 and not end:
                        round_x(q + 1)
                    if first and i == 2 and not end:
                        low_x(q + 1)
                    if i >= 2 and not (first and not end):
                        turn_strips(b, q + 1, i - 2, begins=first)
                    if i == 3 and not first:
                        add_group(b, q * 2 + 1, 1)

            for q in range(QUARTERS):
                if q == 1:
                    dve.wait_ge(t_loaded, 16)
                    nc.vector.tensor_scalar(neg_t[:], t_col[:], T_MIN, -1.0, ALU.max, ALU.mult)\
                        .then_inc(neg_t_ready, 1)
                quarter(0, q, True, False, q == QUARTERS - 1)
            dve.wait_ge(coef_ready, 1)
            with dve.Fori(1, BLOCKS - 1) as b:
                begin(b, False)
                with dve.Fori(0, QUARTERS - 1) as q:
                    quarter(b, q, False, False, False)
                quarter(b, QUARTERS - 1, False, False, True)
            begin(BLOCKS - 1, False)
            with dve.Fori(0, QUARTERS - 1) as q:
                quarter(BLOCKS - 1, q, False, True, False)
            quarter(BLOCKS - 1, QUARTERS - 1, False, True, True)
            make_y(BLOCKS)
            split_y(BLOCKS)
            add_group(BLOCKS - 1, GROUPS - 1, 1)

            def turn_odd(o, k):
                dve.wait_ge((c_loaded if o % 2 else b_loaded)[k],
                            (o // 2 + 1 if o % 2 else (BLOCKS - 1) * 4 + o // 2 + 1) * (16 * P // SQ))
                dve.wait_ge(bt_lo_ready[k], (BLOCKS - 1) * 4 + o)
                nc.vector.transpose(b_sq[:, k].rearrange("p j (s n) -> p s j n", n=SQ),
                                    strips_slot(o, k).rearrange("p (s n j) -> p s j n", j=JT, n=SQ))\
                    .then_inc(b_turned, 1)

            def odd_lo(o):
                if o in GPSIMD_LO:
                    return
                dve.wait_ge(bt_hi_ready, (BLOCKS - 1) * 8 + o * 2 + 2)
                hi, lo = odd_parts(o)
                nc.vector.tensor_tensor(lo[:, :, PAIR:], b_sq[:, 1], hi[:, :, PAIR:].bitcast(F32),
                                        ALU.subtract).then_inc(bt_lo_ready[1], 1)

            def add_last(s):
                dve.wait_ge(group_done, (BLOCKS - 1) * GROUPS + s + 1)
                dve.wait_ge(group_added, BLOCKS * GROUPS)
                g = LAST_ORDER[s]
                sums = outT[:, g * GROUP:(g + 1) * GROUP]
                nc.vector.tensor_tensor(sums, sums, ps_out[:, s % 2], ALU.add).then_inc(group_added, 1)

            def row_stats(g):
                dve.wait_ge(rows_turned, g + 1)
                if g >= 1:
                    dve.wait_ge(mean_ready, g)
                for m in range(4):
                    s = nc.vector.bn_stats(stat6[:, m, :], final_bank(g)[:, m * C:(m + 1) * C])
                s.then_inc(stats_ready, 1)

            def row_mean_var(g):
                dve.wait_ge(stats_ready, g + 1)
                for m in range(4):
                    s = nc.vector.bn_aggr(mean_var[:, g % 2, m, :], stat6[:, m, :])
                s.then_inc(mean_ready, 1)

            def row_rstd(g):
                dve.wait_ge(std_ready, g + 1)
                if g >= 2:
                    dve.wait_ge(normed, g - 1)
                nc.vector.reciprocal(rstd[:, g % 2], std[:, g % 2]).then_inc(rstd_ready, 1)

            def row_shift(g):
                dve.wait_ge(rstd_ready, g + 1)
                nc.vector.scalar_tensor_tensor(out=shift[:, g % 2], in0=mean_var[:, g % 2, :, 0], scalar=-1.0,
                                               in1=rstd[:, g % 2], op0=ALU.mult, op1=ALU.mult)\
                    .then_inc(norm_ready, 1)

            odd_lo(0)
            turn_odd(1, 0)
            turn_odd(1, 1)
            for s in range(GROUPS + 1):
                if s < GROUPS:
                    add_last(s)
                if s == 5:
                    odd_lo(3)
                if s >= 1:
                    row_stats(s - 1)
                if s >= 2:
                    row_rstd(s - 2)
                if s >= 1:
                    row_mean_var(s - 1)
                if s >= 2:
                    row_shift(s - 2)
                for o, k in {1: [(2, 0)], 2: [(2, 1), (3, 0)], 3: [(3, 1)]}.get(s, []):
                    turn_odd(o, k)
            row_rstd(GROUPS - 1)
            row_shift(GROUPS - 1)
            s = GROUPS - 1
            dve.wait_ge(norm_ready, s + 1)
            dve.wait_ge(stored[s % ROW_SLOTS], 16 * (s // ROW_SLOTS))
            for m in range(4):
                row = nc.vector.tensor_scalar(rows(s)[:, m * C:(m + 1) * C], final_bank(s)[:, m * C:(m + 1) * C],
                                              rstd[:, s % 2, m:m + 1], shift[:, s % 2, m:m + 1],
                                              ALU.mult, ALU.add)
            row.then_inc(last_normed, 1)

        @block.tensor
        def _(pe):
            pe.wait_ge(identity_ready, 1)

            def turn_pair(i):
                for n in range(2):
                    tile = k_tiles(raw[:, i, n * KB:(n + 1) * KB])
                    for j in range(JT):
                        last = nc.tensor.transpose(ps_t[:, i, j, n * P:(n + 1) * P], tile[:, j], ident[:])
                last.then_inc(turned[i], 1)

            def spectrum(b, q, i):
                count = b * 16 + q * 4 + (i + 1)
                if isinstance(b, int) and b == 0:
                    pe.wait_ge(x_lo_ready, q + 1)
                pe.wait_ge(lo_v_ready, count)
                pe.wait_ge(lo_g_ready, count)
                hi, lo = a_slot(i, isinstance(b, int) and b == 0)
                for n in range(2):
                    tile = slice((q * 8 + i * 2 + n) * P, (q * 8 + i * 2 + n + 1) * P)
                    cols = slice(n * KB, (n + 1) * KB)
                    opens = q == 0 and i == 0 and n == 0
                    closes = q == QUARTERS - 1 and i == 3 and n == 1
                    nc.tensor.matmul(ps_spec[:], x_hi[:, tile], hi[:, cols], start=opens, stop=False)
                    nc.tensor.matmul(ps_spec[:], x_hi[:, tile], lo[:, cols], start=False, stop=False)
                    last = nc.tensor.matmul(ps_spec[:], x_lo[:, tile], hi[:, cols], start=False, stop=closes)
                last.then_inc(spec_done, 1)

            def synthesis_half(b, q, h, step=None):
                odd, half = h // 2, h % 2
                step = q * 2 + odd if step is None else step
                bank = step % 2
                if half == 0:
                    pe.wait_ge(group_added, b * GROUPS + step - 1)
                    pe.wait_ge(y_hi_ready, b)
                    if odd:
                        for k in range(2):
                            pe.wait_ge(bt_lo_ready[k], b * 4 + q - 3)
                    else:
                        pe.wait_ge(at_lo_ready, b * 8 + q * 2 - 6)
                if odd:
                    hi, lo = odd_parts(q if isinstance(b, int) and b == BLOCKS else 0)
                else:
                    hi, lo = (m[:, :, q * GROUP:(q + 1) * GROUP] for m in (at_hi, at_lo))
                js = range(2 * half, 2 * half + 2)
                for j in js:
                    nc.tensor.matmul(ps_out[:, bank], y_hi[:, y_slot(b), j], hi[:, j], start=j == 0, stop=False)
                    nc.tensor.matmul(ps_out[:, bank], y_hi[:, y_slot(b), j], lo[:, j], start=False, stop=False)
                if half == 0:
                    pe.wait_ge(y_ready, b)
                for j in js:
                    product = nc.tensor.matmul(ps_out[:, bank], y_lo[:, y_slot(b), j], hi[:, j], start=False,
                                               stop=j == JT - 1)
                if half == 1:
                    product.then_inc(group_done, 1)

            def turn_spectrum(b):
                pe.wait_ge(xspec_ready, b)
                for j in range(JT):
                    last = nc.tensor.transpose(ps_y[:, j], k_tiles(xspec[:])[:, j], ident[:])
                last.then_inc(xspec_turned, 1)

            def turn_x(n):
                if n:
                    pe.wait_ge(group_added, 2 * n)
                for k in range(2):
                    for m in range(4):
                        lo = (k * 4 + m) * C
                        last = nc.tensor.transpose(ps_out[:, k, m * P:(m + 1) * P], x_stage[n][:, lo:lo + C],
                                                   ident[:])
                    last.then_inc(x_turned, 1)

            def keep_awake(times):
                for _ in range(times):
                    nc.tensor.transpose(ps_y[:, 0], ident[:], ident[:])

            keep_awake(WARM[0])
            pe.wait_ge(raw_loaded[0], 16)
            turn_pair(0)
            keep_awake(WARM[1])

            def quarter(b, q, first, last, end):
                for i in range(4):
                    if i == 0 and q > 0:
                        spectrum(b, q, i)
                    if i == 0:
                        pe.wait_ge(raw_loaded[1], (b * QUARTERS + q + 1) * 16)
                        if not (first and q == 0):
                            pe.wait_ge(at_lo_ready, b * 8 + q * 2)
                        turn_pair(1)
                    if i == 0 and q == 0:
                        if not first:
                            turn_spectrum(b)
                        spectrum(b, q, i)
                    if i > 0:
                        spectrum(b, q, i)
                    if first and i == 0:
                        pe.wait_ge(x_loaded[q], 16)
                        turn_x(q)
                    if not first:
                        if last and end and i >= 2:
                            halves = [] if i == 2 else [2]
                        else:
                            halves = [i] if q or i > 1 else [[], [0, 1]][i]
                        for h in halves:
                            synthesis_half(b, q, h)
                    if i == 3 and not (last and end):
                        pe.wait_ge(raw_loaded[0], (b * QUARTERS + q + 2) * 16)
                        pe.wait_ge(at_lo_ready, b * 8 + q * 2 + 1)
                        turn_pair(0)

            for q in range(QUARTERS):
                quarter(0, q, True, False, q == QUARTERS - 1)
            with pe.Fori(1, BLOCKS - 1) as b:
                for q in range(QUARTERS):
                    quarter(b, q, False, False, q == QUARTERS - 1)
            for q in range(QUARTERS):
                quarter(BLOCKS - 1, q, False, True, q == QUARTERS - 1)
            turn_spectrum(BLOCKS)
            synthesis_half(BLOCKS - 1, QUARTERS - 1, 3)

            def turn_rows(s):
                pe.wait_ge(group_added, BLOCKS * GROUPS + s + 1)
                if s >= 4:
                    pe.wait_ge(normed, s - 3)
                for m in range(4):
                    lo = LAST_ORDER[s] * GROUP + m * P
                    last = nc.tensor.transpose(final_bank(s)[:, m * P:(m + 1) * P], outT[:, lo:lo + P], ident[:])
                last.then_inc(rows_turned, 1)

            for s in range(GROUPS):
                g = LAST_ORDER[s]
                for half in range(2):
                    synthesis_half(BLOCKS, g // 2, 2 * (g % 2) + half, step=s)
                if s >= 1:
                    turn_rows(s - 1)
            turn_rows(GROUPS - 1)


_INS = ["x", "adj", "L0_gnn_evals", "L0_gnn_t"]


def kernel(**inputs):
    import numpy as np
    import concourse.bacc as bacc
    from concourse.bass_utils import run_bass_kernel_spmd

    nc = bacc.Bacc("TRN2", target_bir_lowering=False, num_devices=1)
    arrays, args = {}, []
    for name in _INS:
        a = np.ascontiguousarray(inputs[name])
        arrays[f"in_{name}"] = a
        args.append(nc.dram_tensor(f"in_{name}", a.shape, mybir.dt.from_np(a.dtype), kind="ExternalInput").ap())
    result = nc.dram_tensor("out_0", (N, C), F32, kind="ExternalOutput").ap()
    build(nc, *args, result)
    return run_bass_kernel_spmd(nc, [arrays], core_ids=[0]).results[0]["out_0"]
```
